# Optimizing a Trainium2 kernel written in Bass

```python
import numpy as np
import jax
import jax.numpy as jnp

def _softmax(x, axis=-1):
    return jax.nn.softmax(x, axis=axis)

def _gelu(x):
    return jax.nn.gelu(x, approximate=True)

def _silu(x):
    return jax.nn.silu(x)

def _sigmoid(x):
    return jax.nn.sigmoid(x)

def _layernorm(x, axis=-1, eps=1e-05):
    m = jnp.mean(x, axis=axis, keepdims=True)
    v = jnp.var(x, axis=axis, keepdims=True)
    return (x - m) / jnp.sqrt(v + eps)

def _scatter_add(tgt, idx, src, axis=0):
    return tgt.at[idx].add(src)

def _segment_sum(src, seg, n):
    return jax.ops.segment_sum(src, seg, n)
kernel_name = 'mk_dlrm_tower_d1_rec_r8_2349a2'

def setup_inputs(seed: int=0):
    np.random.seed(seed)
    _w = jnp.asarray

    def _rec_inputs():
        import jax
        import jax.numpy as jnp
        _tk = jax.random.key(seed)
        ids = jnp.stack([jax.random.randint(jax.random.fold_in(_tk, 200 + f), (512,), 0, v, jnp.int32) for f, v in enumerate([125000, 12500, 1250, 1250, 12500, 1000, 1000, 1000, 1250, 12500, 12500, 1250, 12500, 12500, 1250, 12500, 1000, 1250, 12500, 1000, 1250, 1250, 1250, 1250, 1000, 1250])], axis=1)
        tbl_0 = 0.05 * jax.random.normal(jax.random.fold_in(_tk, 500 + 0), (125000, 128), jnp.float32)
        tbl_1 = 0.05 * jax.random.normal(jax.random.fold_in(_tk, 500 + 1), (12500, 128), jnp.float32)
        tbl_2 = 0.05 * jax.random.normal(jax.random.fold_in(_tk, 500 + 2), (1250, 128), jnp.float32)
        tbl_3 = 0.05 * jax.random.normal(jax.random.fold_in(_tk, 500 + 3), (1250, 128), jnp.float32)
        tbl_4 = 0.05 * jax.random.normal(jax.random.fold_in(_tk, 500 + 4), (12500, 128), jnp.float32)
        tbl_5 = 0.05 * jax.random.normal(jax.random.fold_in(_tk, 500 + 5), (1000, 128), jnp.float32)
        tbl_6 = 0.05 * jax.random.normal(jax.random.fold_in(_tk, 500 + 6), (1000, 128), jnp.float32)
        tbl_7 = 0.05 * jax.random.normal(jax.random.fold_in(_tk, 500 + 7), (1000, 128), jnp.float32)
        tbl_8 = 0.05 * jax.random.normal(jax.random.fold_in(_tk, 500 + 8), (1250, 128), jnp.float32)
        tbl_9 = 0.05 * jax.random.normal(jax.random.fold_in(_tk, 500 + 9), (12500, 128), jnp.float32)
        tbl_10 = 0.05 * jax.random.normal(jax.random.fold_in(_tk, 500 + 10), (12500, 128), jnp.float32)
        tbl_11 = 0.05 * jax.random.normal(jax.random.fold_in(_tk, 500 + 11), (1250, 128), jnp.float32)
        tbl_12 = 0.05 * jax.random.normal(jax.random.fold_in(_tk, 500 + 12), (12500, 128), jnp.float32)
        tbl_13 = 0.05 * jax.random.normal(jax.random.fold_in(_tk, 500 + 13), (12500, 128), jnp.float32)
        tbl_14 = 0.05 * jax.random.normal(jax.random.fold_in(_tk, 500 + 14), (1250, 128), jnp.float32)
        tbl_15 = 0.05 * jax.random.normal(jax.random.fold_in(_tk, 500 + 15), (12500, 128), jnp.float32)
        tbl_16 = 0.05 * jax.random.normal(jax.random.fold_in(_tk, 500 + 16), (1000, 128), jnp.float32)
        tbl_17 = 0.05 * jax.random.normal(jax.random.fold_in(_tk, 500 + 17), (1250, 128), jnp.float32)
        tbl_18 = 0.05 * jax.random.normal(jax.random.fold_in(_tk, 500 + 18), (12500, 128), jnp.float32)
        tbl_19 = 0.05 * jax.random.normal(jax.random.fold_in(_tk, 500 + 19), (1000, 128), jnp.float32)
        tbl_20 = 0.05 * jax.random.normal(jax.random.fold_in(_tk, 500 + 20), (1250, 128), jnp.float32)
        tbl_21 = 0.05 * jax.random.normal(jax.random.fold_in(_tk, 500 + 21), (1250, 128), jnp.float32)
        tbl_22 = 0.05 * jax.random.normal(jax.random.fold_in(_tk, 500 + 22), (1250, 128), jnp.float32)
        tbl_23 = 0.05 * jax.random.normal(jax.random.fold_in(_tk, 500 + 23), (1250, 128), jnp.float32)
        tbl_24 = 0.05 * jax.random.normal(jax.random.fold_in(_tk, 500 + 24), (1000, 128), jnp.float32)
        tbl_25 = 0.05 * jax.random.normal(jax.random.fold_in(_tk, 500 + 25), (1250, 128), jnp.float32)
        _rk = jax.random.fold_in(_tk, 7)
        r_dense_features = -0.000520686 + 1.00062 * jax.random.normal(jax.random.fold_in(_rk, 101), (512, 128), jnp.float32)
        W_top1 = 0.0405887 * jax.random.normal(jax.random.fold_in(_tk, 801), (607, 512), jnp.float32)
        W_top2 = 0.0441942 * jax.random.normal(jax.random.fold_in(_tk, 802), (512, 256), jnp.float32)
        W_top3 = 0.0625 * jax.random.normal(jax.random.fold_in(_tk, 803), (256, 1), jnp.float32)
        b_top1 = jnp.zeros((512,), jnp.float32)
        b_top2 = jnp.zeros((256,), jnp.float32)
        return (r_dense_features, ids, tbl_0, tbl_1, tbl_2, tbl_3, tbl_4, tbl_5, tbl_6, tbl_7, tbl_8, tbl_9, tbl_10, tbl_11, tbl_12, tbl_13, tbl_14, tbl_15, tbl_16, tbl_17, tbl_18, tbl_19, tbl_20, tbl_21, tbl_22, tbl_23, tbl_24, tbl_25, W_top1, b_top1, W_top2, b_top2, W_top3)
    r_dense_features, ids, tbl_0, tbl_1, tbl_2, tbl_3, tbl_4, tbl_5, tbl_6, tbl_7, tbl_8, tbl_9, tbl_10, tbl_11, tbl_12, tbl_13, tbl_14, tbl_15, tbl_16, tbl_17, tbl_18, tbl_19, tbl_20, tbl_21, tbl_22, tbl_23, tbl_24, tbl_25, W_top1, b_top1, W_top2, b_top2, W_top3 = _rec_inputs()

    def _L0_rec_setup():
        import jax, jax.numpy as jnp
        import numpy as np
        B, F, D = (2048, 26, 128)
        key = jax.random.key(seed)
        k1, k2 = jax.random.split(key)
        dense_features = jax.random.normal(k1, (B, D), dtype=jnp.float32)
        sparse_values = jax.random.normal(k2, (B, F, D), dtype=jnp.float32)
        return {'dense_features': dense_features, 'sparse_values': sparse_values}
    _L0_rec_all = _L0_rec_setup()
    _L0_rec_in = {k: v for k, v in _L0_rec_all.items() if k in ()}
    del _L0_rec_all
    return {'r_dense_features': r_dense_features, 'ids': ids, 'tbl_0': tbl_0, 'tbl_1': tbl_1, 'tbl_2': tbl_2, 'tbl_3': tbl_3, 'tbl_4': tbl_4, 'tbl_5': tbl_5, 'tbl_6': tbl_6, 'tbl_7': tbl_7, 'tbl_8': tbl_8, 'tbl_9': tbl_9, 'tbl_10': tbl_10, 'tbl_11': tbl_11, 'tbl_12': tbl_12, 'tbl_13': tbl_13, 'tbl_14': tbl_14, 'tbl_15': tbl_15, 'tbl_16': tbl_16, 'tbl_17': tbl_17, 'tbl_18': tbl_18, 'tbl_19': tbl_19, 'tbl_20': tbl_20, 'tbl_21': tbl_21, 'tbl_22': tbl_22, 'tbl_23': tbl_23, 'tbl_24': tbl_24, 'tbl_25': tbl_25, 'W_top1': W_top1, 'b_top1': b_top1, 'W_top2': W_top2, 'b_top2': b_top2, 'W_top3': W_top3}

def reference(r_dense_features, ids, tbl_0, tbl_1, tbl_2, tbl_3, tbl_4, tbl_5, tbl_6, tbl_7, tbl_8, tbl_9, tbl_10, tbl_11, tbl_12, tbl_13, tbl_14, tbl_15, tbl_16, tbl_17, tbl_18, tbl_19, tbl_20, tbl_21, tbl_22, tbl_23, tbl_24, tbl_25, W_top1, b_top1, W_top2, b_top2, W_top3):
    import jax
    import jax.numpy as jnp

    def _L0_rec_ref(dense_features, sparse_values):
        import jax, jax.numpy as jnp
        import numpy as np
        B, F, D = (2048, 26, 128)
        sd = jnp.einsum('bfd,bd->bf', sparse_values, dense_features)
        ss = jnp.einsum('bfd,bgd->bfg', sparse_values, sparse_values)
        iu, ju = jnp.triu_indices(F, k=1)
        pairs = ss[:, iu, ju]
        return jnp.concatenate([dense_features, sd, pairs], axis=1)
    e = jnp.stack([tbl_0[ids[:, 0]], tbl_1[ids[:, 1]], tbl_2[ids[:, 2]], tbl_3[ids[:, 3]], tbl_4[ids[:, 4]], tbl_5[ids[:, 5]], tbl_6[ids[:, 6]], tbl_7[ids[:, 7]], tbl_8[ids[:, 8]], tbl_9[ids[:, 9]], tbl_10[ids[:, 10]], tbl_11[ids[:, 11]], tbl_12[ids[:, 12]], tbl_13[ids[:, 13]], tbl_14[ids[:, 14]], tbl_15[ids[:, 15]], tbl_16[ids[:, 16]], tbl_17[ids[:, 17]], tbl_18[ids[:, 18]], tbl_19[ids[:, 19]], tbl_20[ids[:, 20]], tbl_21[ids[:, 21]], tbl_22[ids[:, 22]], tbl_23[ids[:, 23]], tbl_24[ids[:, 24]], tbl_25[ids[:, 25]]], axis=1)
    z = _L0_rec_ref(r_dense_features, e)
    z = z.reshape(z.shape[0], -1)
    h = jnp.concatenate([z, r_dense_features], axis=1)
    h = jnp.maximum(h @ W_top1 + b_top1, 0.0)
    h = jnp.maximum(h @ W_top2 + b_top2, 0.0)
    y = h @ W_top3
    return y

_drawn_inputs = setup_inputs


def setup_inputs(seed=0):
    import zlib

    import numpy as np

    out = dict(_drawn_inputs(seed))
    spreads = {'b_top1': (0.0, 0.1), 'b_top2': (0.0, 0.1)}
    factors = {}
    for name, (base, spread) in spreads.items():
        noise = np.random.default_rng([zlib.crc32(name.encode()), seed]).standard_normal(out[name].shape)
        drawn = base * np.exp(spread * noise) if base else spread * noise
        out[name] = jnp.asarray(drawn.astype(out[name].dtype))
    for name, factor in factors.items():
        out[name] = (out[name] * factor).astype(out[name].dtype)
    return out
```

```python
from contextlib import ExitStack

import concourse.bass as bass
from concourse import mybir

F32 = mybir.dt.float32
I32 = mybir.dt.int32
ALU = mybir.AluOpType
ACT = mybir.ActivationFunctionType

P = 128
BATCH, D, FIELDS = 512, 128, 26
H1, H2 = 512, 256
TILES = BATCH // P
SLOTS = FIELDS + 1
PITCH = 32
QUADS = P // PITCH
GROUPS = P // QUADS
HALF = GROUPS // 2
BANK = 512
COLS = QUADS * FIELDS
PER_BANK = BANK // COLS
GRAM_BANKS = HALF // PER_BANK
STEPS = -(-FIELDS // QUADS)
BATCHES = [(g, min(4, FIELDS - g)) for g in range(0, FIELDS, 4)]
NB = len(BATCHES)
NB_DVE, NB_ACT = len(BATCHES[0::2]), len(BATCHES[1::2])
OC1, OC2 = H1 // P, H2 // P


def build(nc, ins, out):
    with ExitStack() as ctx:
        def sb(name, shape, dt=F32):
            return ctx.enter_context(nc.sbuf_tensor(name, shape, dt))

        def sem(name):
            return ctx.enter_context(nc.semaphore(name))

        ids = sb("ids_sb", [P, TILES, FIELDS], I32)
        dense = sb("dense", [P, TILES, D])
        ident = sb("ident", [P, P])
        rows = sb("rows", [P, FIELDS, D])
        dense_t = sb("dense_t", [P, BATCH])
        vecs = sb("vecs", [P, P, PITCH])
        dots = sb("dots", [P, STEPS, P])
        w1_dense = sb("w1_dense", [P, 2, H1])
        w1_fold = sb("w1_fold", [P, H1])
        w1_dots = sb("w1_dots", [P, STEPS, H1])
        w2 = sb("w2", [P, OC1, H2])
        w3 = sb("w3", [P, OC2])
        b1 = sb("b1", [P, OC1])
        b2 = sb("b2", [P, OC2])
        h1 = sb("h1", [P, OC1, P])
        h2 = sb("h2", [P, OC2, P])
        y = sb("y", [P, TILES])

        ps_dve = ctx.enter_context(nc.psum_tensor("ps_dve", [P, 4, P], F32))
        ps_act = ctx.enter_context(nc.psum_tensor("ps_act", [P, 4, P], F32))
        ps_gram = ctx.enter_context(nc.psum_tensor("ps_gram", [P, GRAM_BANKS, BANK], F32))
        ps_h_dve = ctx.enter_context(nc.psum_tensor("ps_h_dve", [P, BANK], F32))
        ps_h_act = ctx.enter_context(nc.psum_tensor("ps_h_act", [P, BANK], F32))

        s_ids = sem("s_ids")
        s_dense = sem("s_dense")
        s_w1 = sem("s_w1")
        s_w2 = sem("s_w2")
        s_zero = sem("s_zero")
        s_ident = sem("s_ident")
        s_pad = sem("s_pad")
        s_fold = sem("s_fold")
        s_rows = [sem(f"s_rows{g}") for g in range(NB)]
        s_dense_tp = sem("s_dense_tp")
        s_tp = sem("s_tp")
        s_dve_read = sem("s_dve_read")
        s_act_read = sem("s_act_read")
        s_slot0 = sem("s_slot0")
        s_gram = sem("s_gram")
        s_fold_dve = sem("s_fold_dve")
        s_fold_act = sem("s_fold_act")
        s_h1 = sem("s_h1")
        s_h2 = sem("s_h2")
        s_y = sem("s_y")
        s_h_dve_read = sem("s_h_dve_read")
        s_h_act_read = sem("s_h_act_read")
        s_out = sem("s_out")

        def wait_reuse(eng, s, count):
            if not (isinstance(count, int) and count == 0):
                eng.wait_ge(s, count)

        def gram_block(s, q):
            steps = len(range(q, FIELDS, QUADS))
            src = ps_gram[PITCH * s:PITCH * (s + 1), :, 0:PER_BANK * COLS].rearrange(
                "a k (g c) -> a k g c", g=PER_BANK)
            return src[:, :, :, s * FIELDS + q:(s + 1) * FIELDS:QUADS], steps

        def dots_block(s, q, half, steps):
            dst = dots[PITCH * q:PITCH * (q + 1), 0:steps, :].rearrange(
                "a j (h k g s) -> a h s k g j", h=2, k=GRAM_BANKS, g=PER_BANK)
            return dst[:, half, s]

        def vecs_block(g0, n):
            return vecs[:, :, 1 + g0:1 + g0 + n].rearrange("d p f -> d f p")

        block = ctx.enter_context(nc.Block())

        @block.sync
        def _(sp):
            sp.dma_start(ids[:, :, :], ins["ids"].rearrange("(p t) f -> p t f", t=TILES)).then_inc(s_ids, 16)
            sp.dma_start(dense[:, :, :], ins["r_dense_features"].rearrange("(p t) d -> p t d", t=TILES)
                         ).then_inc(s_dense, 16)
            sp.dma_start(w1_dense[:, :, :], ins["w1_dense"]).then_inc(s_w1, 16)
            sp.dma_start(w1_dots[:, :, :], ins["w1_dots"]).then_inc(s_w1, 16)
            sp.dma_start(b1[:, :], ins["b_top1"]).then_inc(s_w1, 16)
            sp.dma_start(w2[:, :, :], ins["W_top2"]).then_inc(s_w2, 16)
            sp.dma_start(b2[:, :], ins["b_top2"]).then_inc(s_w2, 16)
            sp.dma_start(w3[:, :], ins["W_top3"]).then_inc(s_w2, 16)
            sp.wait_ge(s_h_dve_read, TILES * 3)
            sp.dma_start(out.rearrange("(p t) o -> p (t o)", t=TILES), y[:, :]).then_inc(s_out, 16)
            sp.wait_ge(s_out, 16)

        @block.gpsimd
        def _(pool):
            nc.gpsimd.memset(ident[:, :], 0.0).then_inc(s_zero, 1)
            pool.wait_ge(s_zero, 1)
            nc.gpsimd.affine_select(out=ident[:, :], in_=ident[:, :], compare_op=ALU.not_equal, fill=1.0,
                                    base=0, pattern=[[-1, P]], channel_multiplier=1).then_inc(s_ident, 1)
            pool.wait_ge(s_ids, 16)

            for t in range(TILES):
                for g, (f0, n) in enumerate(BATCHES):
                    if t >= 1:
                        pool.wait_ge(s_tp, (t - 1) * NB + g + 1)
                    for f in range(f0, f0 + n):
                        pool.indirect_dma_start(
                            out=rows[:, f, :], out_offset=None, in_=ins[f"tbl_{f}"],
                            in_offset=bass.IndirectOffsetOnAxis(ap=ids[:, t, f:f + 1], axis=0),
                        ).then_inc(s_rows[g], 16)

        @block.tensor
        def _(pe):
            pe.wait_ge(s_ident, 1)
            pe.wait_ge(s_dense, 16)
            for t in range(TILES):
                last = pe.transpose(ps_dve[:, t, :], dense[:, t, :], ident[:, :])
            last.then_inc(s_dense_tp, 1)
            pe.wait_ge(s_w1, 48)
            pe.wait_ge(s_w2, 48)
            pe.wait_ge(s_fold, 1)
            pe.wait_ge(s_pad, 1)
            def pe_tile(t):
                for g, (f0, n) in enumerate(BATCHES):
                    pe.wait_ge(s_rows[g], t * (16 * n) + 16 * n)
                    if g % 2 == 0:
                        ps = ps_dve
                        pe.wait_ge(s_dve_read, t * (NB_DVE + 1) + (1 + g // 2))
                    else:
                        ps = ps_act
                        wait_reuse(pe, s_act_read, t * (NB_ACT + 1) + g // 2)
                    for k in range(n):
                        last = pe.transpose(ps[:, k, :], rows[:, f0 + k, :], ident[:, :])
                    last.then_inc(s_tp, 1)

                pe.wait_ge(s_slot0, t + 1)
                pe.wait_ge(s_dve_read, t * (NB_DVE + 1) + (1 + NB_DVE))
                pe.wait_ge(s_act_read, t * (NB_ACT + 1) + NB_ACT)
                for half in range(2):
                    wait_reuse(pe, s_fold_dve, t * 2 + half)
                    wait_reuse(pe, s_fold_act, t * 2 + half)
                    for g in range(HALF):
                        p0 = QUADS * (half * HALF + g)
                        c0 = (g % PER_BANK) * COLS
                        last = pe.matmul(ps_gram[:, g // PER_BANK, c0:c0 + COLS],
                                         vecs[:, p0:p0 + QUADS, :], vecs[:, p0:p0 + QUADS, 1:SLOTS],
                                         start=True, stop=True)
                    last.then_inc(s_gram, 1)

                for o in range(OC1):
                    ps = ps_h_act if o % 2 else ps_h_dve
                    if o % 2:
                        wait_reuse(pe, s_h_act_read, t * 2 + o // 2)
                    else:
                        wait_reuse(pe, s_h_dve_read, t * 3 + o // 2)
                    pe.matmul(ps[:, 0:P], w1_fold[:, o * P:(o + 1) * P],
                              dense_t[:, bass.ds(t * P, P)], start=True, stop=False)
                    if o == 0:
                        pe.wait_ge(s_fold_dve, t * 2 + 2)
                        pe.wait_ge(s_fold_act, t * 2 + 2)
                    for j in range(STEPS):
                        k = PITCH * min(QUADS, FIELDS - QUADS * j)
                        last = pe.matmul(ps[:, 0:P], w1_dots[0:k, j, o * P:(o + 1) * P],
                                         dots[0:k, j, :], start=False, stop=(j == STEPS - 1))
                    last.then_inc(s_h1, 1)

                pe.wait_ge(s_h_dve_read, t * 3 + 2)
                pe.wait_ge(s_h_act_read, t * 2 + 2)
                for o in range(OC2):
                    ps = ps_act if o % 2 else ps_dve
                    for c in range(OC1):
                        last = pe.matmul(ps[:, 0, :], w2[:, c, o * P:(o + 1) * P], h1[:, c, :],
                                         start=(c == 0), stop=(c == OC1 - 1))
                    last.then_inc(s_h2, 1)

                pe.wait_ge(s_dve_read, t * (NB_DVE + 1) + (NB_DVE + 2))
                pe.wait_ge(s_act_read, t * (NB_ACT + 1) + (NB_ACT + 1))
                for c in range(OC2):
                    last = pe.matmul(ps_h_dve[:, 0:1], h2[:, c, :], w3[:, c:c + 1],
                                     start=(c == 0), stop=(c == OC2 - 1))
                last.then_inc(s_y, 1)

            pe_tile(0)
            with pe.Fori(1, TILES) as t:
                pe_tile(t)

        @block.vector
        def _(dve):
            nc.vector.memset(vecs[:, :, SLOTS:PITCH], 0.0).then_inc(s_pad, 1)
            dve.wait_ge(s_w1, 48)
            nc.vector.tensor_add(w1_fold[:, :], w1_dense[:, 0, :], w1_dense[:, 1, :]).then_inc(s_fold, 1)
            dve.wait_ge(s_dense_tp, 1)
            nc.vector.tensor_copy(dense_t[:, :], ps_dve[:, :, :].rearrange("d t p -> d (t p)")
                                  ).then_inc(s_dve_read, 1)
            dve.wait_ge(s_w2, 48)
            def dve_tile(t):
                for g, (f0, n) in list(enumerate(BATCHES))[0::2]:
                    dve.wait_ge(s_tp, t * NB + (g + 1))
                    nc.vector.tensor_copy(vecs_block(f0, n), ps_dve[:, 0:n, :]).then_inc(s_dve_read, 1)
                for half in range(2):
                    dve.wait_ge(s_gram, t * 2 + (half + 1))
                    for s in range(0, QUADS // 2):
                        for q in range(QUADS):
                            src, steps = gram_block(s, q)
                            last = nc.vector.tensor_copy(dots_block(s, q, half, steps), src)
                    last.then_inc(s_fold_dve, 1)
                for o in range(0, OC1, 2):
                    dve.wait_ge(s_h1, t * OC1 + (o + 1))
                    nc.vector.tensor_scalar(h1[:, o, :], ps_h_dve[:, 0:P], b1[:, o:o + 1], 0.0,
                                            ALU.add, ALU.max).then_inc(s_h_dve_read, 1)
                dve.wait_ge(s_h2, t * OC2 + 1)
                nc.vector.tensor_scalar(h2[:, 0, :], ps_dve[:, 0, :], b2[:, 0:1], 0.0,
                                        ALU.add, ALU.max).then_inc(s_dve_read, 1)
                dve.wait_ge(s_y, t + 1)
                nc.vector.tensor_copy(y[:, bass.ds(t, 1)], ps_h_dve[:, 0:1]).then_inc(s_h_dve_read, 1)

            dve_tile(0)
            with dve.Fori(1, TILES) as t:
                dve_tile(t)

        @block.scalar
        def _(act):
            act.wait_ge(s_dve_read, 1)
            act.wait_ge(s_w1, 48)
            act.wait_ge(s_w2, 48)
            def act_tile(t):
                wait_reuse(act, s_gram, t * 2)
                nc.scalar.copy(vecs[:, :, 0:1].rearrange("d p f -> d (p f)"), dense_t[:, bass.ds(t * P, P)]).then_inc(s_slot0, 1)
                for g, (f0, n) in list(enumerate(BATCHES))[1::2]:
                    act.wait_ge(s_tp, t * NB + (g + 1))
                    nc.scalar.copy(vecs_block(f0, n), ps_act[:, 0:n, :]).then_inc(s_act_read, 1)
                for half in range(2):
                    act.wait_ge(s_gram, t * 2 + (half + 1))
                    for s in range(QUADS // 2, QUADS):
                        for q in range(QUADS):
                            src, steps = gram_block(s, q)
                            last = nc.scalar.copy(dots_block(s, q, half, steps), src)
                    last.then_inc(s_fold_act, 1)
                for o in range(1, OC1, 2):
                    act.wait_ge(s_h1, t * OC1 + (o + 1))
                    nc.scalar.activation(h1[:, o, :], ps_h_act[:, 0:P], ACT.Relu,
                                         bias=b1[:, o:o + 1]).then_inc(s_h_act_read, 1)
                act.wait_ge(s_h2, t * OC2 + 2)
                nc.scalar.activation(h2[:, 1, :], ps_act[:, 0, :], ACT.Relu,
                                     bias=b2[:, 1:2]).then_inc(s_act_read, 1)

            act_tile(0)
            with act.Fori(1, TILES) as t:
                act_tile(t)


def lay_out(inputs):
    import numpy as np

    arrays = {n: np.ascontiguousarray(inputs[n])
              for n in ["r_dense_features", "ids"] + [f"tbl_{f}" for f in range(FIELDS)]}
    w1 = np.asarray(inputs["W_top1"])
    pairs = w1[D:D + SLOTS * (SLOTS - 1) // 2]
    arrays["w1_dense"] = np.ascontiguousarray(np.stack([w1[:D], w1[-D:]], axis=1))
    w1_dots = np.zeros((P, STEPS, H1), w1.dtype)
    for row, (a, b) in enumerate((a, b) for a in range(SLOTS) for b in range(a + 1, SLOTS)):
        j, q = divmod(b - 1, QUADS)
        w1_dots[PITCH * q + a, j] = pairs[row]
    arrays["w1_dots"] = w1_dots
    arrays["b_top1"] = np.ascontiguousarray(np.asarray(inputs["b_top1"]).reshape(OC1, P).T)
    arrays["b_top2"] = np.ascontiguousarray(np.asarray(inputs["b_top2"]).reshape(OC2, P).T)
    arrays["W_top2"] = np.ascontiguousarray(np.asarray(inputs["W_top2"]).reshape(OC1, P, H2).transpose(1, 0, 2))
    arrays["W_top3"] = np.ascontiguousarray(np.asarray(inputs["W_top3"]).reshape(OC2, P).T)
    return arrays


def kernel(**inputs):
    import concourse.bacc as bacc
    from concourse.bass_utils import run_bass_kernel_spmd

    nc = bacc.Bacc("TRN2", target_bir_lowering=False, num_devices=1)
    arrays = lay_out(inputs)
    ins = {n: nc.dram_tensor(f"in_{n}", a.shape, mybir.dt.from_np(a.dtype), kind="ExternalInput").ap()
           for n, a in arrays.items()}
    out = nc.dram_tensor("out_y", (BATCH, 1), F32, kind="ExternalOutput").ap()
    build(nc, ins, out)
    r = run_bass_kernel_spmd(nc, [{f"in_{n}": a for n, a in arrays.items()}], core_ids=[0])
    return r.results[0]["out_y"]
```

```python
from contextlib import ExitStack

import concourse.bass as bass
from concourse import mybir

F32 = mybir.dt.float32
F32R = mybir.dt.float32r
I32 = mybir.dt.int32
ALU = mybir.AluOpType
ACT = mybir.ActivationFunctionType

P = 128
BATCH, D, FIELDS = 512, 128, 26
H1, H2 = 512, 256
TILES = BATCH // P
SLOTS = FIELDS + 1
PITCH = 32
QUADS = P // PITCH
STEPS = -(-FIELDS // QUADS)
OC1, OC2 = H1 // P, H2 // P

HOT_ROWS = 1000
HOT = [5, 6, 7, 16, 19]
NHOT = len(HOT)
KT = 8
KP = HOT_ROWS // KT
KP_A = KP // 16 * 16
KS_ACT = [[4, 5, 6] if i % 2 == 0 else [4, 5] for i in range(NHOT)]
KS_DVE = [[k for k in range(KT) if k not in KS_ACT[i]] for i in range(NHOT)]
RING = 3
EARLY = 1 + NHOT

SLOT_TABLES = HOT + [f for f in range(FIELDS) if f not in HOT]
COLD = SLOT_TABLES[NHOT:]
BATCHES, _slot = [], EARLY
while _slot < SLOTS:
    _end = min(SLOTS, 1 + QUADS * (-(-_slot // QUADS)))
    BATCHES.append((_slot, _end - _slot))
    _slot = _end
NB = len(BATCHES)
NB_DVE, NB_ACT = len(BATCHES[0::2]), len(BATCHES[1::2])

PAIR = 2
COLS = PAIR * FIELDS
PARTS = 4
PER_PART = P // QUADS // PARTS
BANK = 512
FOLD_DVE, FOLD_ACT = [0, 1], [2, 3]


def build(nc, ins, out):
    with ExitStack() as ctx:
        def sb(name, shape, dt=F32):
            return ctx.enter_context(nc.sbuf_tensor(name, shape, dt))

        def ps(name, shape):
            return ctx.enter_context(nc.psum_tensor(name, shape, F32))

        def sem(name):
            return ctx.enter_context(nc.semaphore(name))

        ids = sb("ids_sb", [P, TILES, FIELDS], I32)
        dense = sb("dense", [P, TILES, D])
        ident = sb("ident", [P, P])
        rows = sb("rows", [P, len(COLD), D])
        early = sb("early", [P, EARLY, BATCH])
        vecs = sb("vecs", [P, P, PITCH])
        dots = sb("dots", [P, STEPS, P])
        w1_dense = sb("w1_dense", [P, 2, H1])
        w1_fold = sb("w1_fold", [P, H1])
        w1_dots = sb("w1_dots", [P, STEPS, H1])
        w2 = sb("w2", [P, OC1, H2])
        w3 = sb("w3", [P, OC2])
        b1 = sb("b1", [P, OC1])
        b2 = sb("b2", [P, OC2])
        h1 = sb("h1", [P, OC1, P])
        h2 = sb("h2", [P, OC2, P])
        y = sb("y", [P, TILES])
        hot_ids = sb("hot_ids", [P, NHOT, BATCH], I32)
        table = sb("table", [P, NHOT, KT, D])
        table_hi = sb("table_hi", [P, NHOT, KT, D], F32R)
        table_lo = sb("table_lo", [P, NHOT, KT, D], F32R)
        row_id = sb("row_id", [P, KT])
        minus_row_id = sb("minus_row_id", [P, KT])
        distance = sb("distance", [P, 3, BATCH])
        one_hot = sb("one_hot", [P, RING, KT, BATCH], F32R)

        ps_dve = ps("ps_dve", [P, 4, P])
        ps_act = ps("ps_act", [P, 4, P])
        ps_gram = ps("ps_gram", [P, PARTS, BANK])
        ps_h_dve = ps("ps_h_dve", [P, OC1 // 2, P])
        ps_h_act = ps("ps_h_act", [P, OC1 // 2, P])
        ps_h2_dve, ps_h2_act = ps_gram[:, 0, 0:P], ps_gram[:, 1, 0:P]
        ps_y = ps_gram[:, 2, 0:1]
        ps_pick = ps_gram[:, 0:2, :]
        ps_ids = ps_gram[:, 2:4, :]

        s_ids = sem("s_ids")
        s_dense = sem("s_dense")
        s_hot_ids = [sem(f"s_hot_ids{i}") for i in range(2)]
        s_table = [sem(f"s_table{i}") for i in range(NHOT)]
        s_w1 = sem("s_w1")
        s_w2 = sem("s_w2")
        s_zero = sem("s_zero")
        s_ident = sem("s_ident")
        s_row_id = sem("s_row_id")
        s_minus = sem("s_minus")
        s_pad = sem("s_pad")
        s_w1_fold = sem("s_w1_fold")
        s_ps_ids = sem("s_ps_ids")
        s_distance = sem("s_distance")
        s_hi = sem("s_hi")
        s_lo = sem("s_lo")
        s_hot_dve = sem("s_hot_dve")
        s_hot_act = sem("s_hot_act")
        s_picked = sem("s_picked")
        s_pick_read = sem("s_pick_read")
        s_rows = [sem(f"s_rows{g}") for g in range(NB)]
        s_dense_tp = sem("s_dense_tp")
        s_tp = sem("s_tp")
        s_dve_read = sem("s_dve_read")
        s_act_read = sem("s_act_read")
        s_early = sem("s_early")
        s_gram = sem("s_gram")
        s_fold_dve = sem("s_fold_dve")
        s_fold_act = sem("s_fold_act")
        s_h1_dve = sem("s_h1_dve")
        s_h1_act = sem("s_h1_act")
        s_h2 = sem("s_h2")
        s_y = sem("s_y")
        s_h_dve_read = sem("s_h_dve_read")
        s_h_act_read = sem("s_h_act_read")
        s_h2_dve_read = sem("s_h2_dve_read")
        s_h2_act_read = sem("s_h2_act_read")
        s_y_read = sem("s_y_read")
        s_out = sem("s_out")

        DENSE_READ = 1

        def wait_reuse(eng, s, count):
            if not (isinstance(count, int) and count <= 0):
                eng.wait_ge(s, count)

        def steps_made(ks, i, n=0):
            return sum(len(x) for x in ks[:i]) + n

        def slots_block(g):
            s0, n = BATCHES[g]
            return vecs[:, :, s0:s0 + n].rearrange("d p f -> d f p")

        def fold_blocks(samples, part):
            src = ps_gram[:, part, 0:PER_PART * COLS].rearrange("a (g s c) -> a g s c", g=PER_PART, s=PAIR)
            dst = dots[:, :, :].rearrange("a j (h g s) -> a h s g j", h=PARTS, g=PER_PART)
            for s in samples:
                for q in range(QUADS):
                    steps = len(range(q, FIELDS, QUADS))
                    yield (dst[PITCH * q:PITCH * (q + 1), part, s, :, 0:steps],
                           src[PITCH * s:PITCH * (s + 1), :, s % PAIR, q:FIELDS:QUADS])

        block = ctx.enter_context(nc.Block())

        @block.sync
        def _(sp):
            def load_table(i):
                whole = ins[f"tbl_{HOT[i]}"].rearrange("(p k) d -> p k d", k=KT)
                sp.dma_start(table[0:KP_A, i], whole[0:KP_A]).then_inc(s_table[i], 16)
                sp.dma_start(table[KP_A:KP, i], whole[KP_A:KP]).then_inc(s_table[i], 16)

            sp.dma_start(ids[:, :, :], ins["ids"].rearrange("(p t) f -> p t f", t=TILES)).then_inc(s_ids, 16)
            sp.dma_start(hot_ids[:, 0, :], ins["hot_ids"][0:1].partition_broadcast(P)).then_inc(s_hot_ids[0], 16)
            load_table(0)
            load_table(1)
            sp.dma_start(hot_ids[:, 1:, :], ins["hot_ids"][1:].partition_broadcast(P)).then_inc(s_hot_ids[1], 16)
            sp.dma_start(dense[:, :, :], ins["r_dense_features"].rearrange("(p t) d -> p t d", t=TILES)
                         ).then_inc(s_dense, 16)
            for i in range(2, NHOT):
                sp.wait_ge(s_hi, i - 1)
                load_table(i)
            sp.wait_ge(s_hi, NHOT - 1)
            sp.dma_start(w1_dense[:, :, :], ins["w1_dense"]).then_inc(s_w1, 16)
            sp.dma_start(w1_dots[:, :, :], ins["w1_dots"]).then_inc(s_w1, 16)
            sp.dma_start(b1[:, :], ins["b_top1"]).then_inc(s_w1, 16)
            sp.dma_start(w2[:, :, :], ins["W_top2"]).then_inc(s_w2, 16)
            sp.dma_start(b2[:, :], ins["b_top2"]).then_inc(s_w2, 16)
            sp.dma_start(w3[:, :], ins["W_top3"]).then_inc(s_w2, 16)
            sp.wait_ge(s_y_read, TILES)
            sp.dma_start(out.rearrange("(p t) o -> p (t o)", t=TILES), y[:, :]).then_inc(s_out, 16)
            sp.wait_ge(s_out, 16)

        @block.gpsimd
        def _(pool):
            nc.gpsimd.memset(ident[:, :], 0.0).then_inc(s_zero, 1)
            nc.gpsimd.iota(row_id[:, :], [[1, KT]], base=0, channel_multiplier=KT,
                           allow_small_or_imprecise_dtypes=True).then_inc(s_row_id, 1)
            pool.wait_ge(s_zero, 1)
            nc.gpsimd.affine_select(out=ident[:, :], in_=ident[:, :], compare_op=ALU.not_equal, fill=1.0,
                                    base=0, pattern=[[-1, P]], channel_multiplier=1).then_inc(s_ident, 1)
            pool.wait_ge(s_ids, 16)
            for t in range(TILES):
                for g, (s0, n) in enumerate(BATCHES):
                    if t >= 1:
                        pool.wait_ge(s_tp, (t - 1) * NB + g + 1)
                    for slot in range(s0, s0 + n):
                        f = SLOT_TABLES[slot - 1]
                        pool.indirect_dma_start(
                            out=rows[:, slot - EARLY, :], out_offset=None, in_=ins[f"tbl_{f}"],
                            in_offset=bass.IndirectOffsetOnAxis(ap=ids[:, t, f:f + 1], axis=0),
                        ).then_inc(s_rows[g], 16)

        @block.tensor
        def _(pe):
            pe.wait_ge(s_ident, 1)
            pe.wait_ge(s_dense, 16)
            for t in range(TILES):
                last = pe.transpose(ps_dve[:, t, :], dense[:, t, :], ident[:, :])
            last.then_inc(s_dense_tp, 1)

            def pick(i):
                pe.wait_ge(s_hi, i + 1)
                if i >= 2:
                    pe.wait_ge(s_pick_read, i - 1)
                for k in range(KT):
                    if k in KS_ACT[i]:
                        pe.wait_ge(s_hot_act, steps_made(KS_ACT, i, KS_ACT[i].index(k) + 1))
                    else:
                        pe.wait_ge(s_hot_dve, steps_made(KS_DVE, i, KS_DVE[i].index(k) + 1))
                    if k == 0:
                        pe.wait_ge(s_lo, i + 1)
                    for part in (table_hi, table_lo):
                        last = pe.matmul(ps_pick[:, i % 2, :], part[0:KP, i, k, :], one_hot[0:KP, i % RING, k, :],
                                         start=(part is table_hi and k == 0), stop=(part is table_lo and k == KT - 1))
                last.then_inc(s_picked, 1)

            def transposes(t, g):
                s0, n = BATCHES[g]
                pe.wait_ge(s_rows[g], t * (16 * n) + 16 * n)
                if g % 2 == 0:
                    bank = ps_dve
                    pe.wait_ge(s_dve_read, t * NB_DVE + (DENSE_READ + g // 2))
                else:
                    bank = ps_act
                    wait_reuse(pe, s_act_read, t * NB_ACT + g // 2)
                for k in range(n):
                    last = pe.transpose(bank[:, k, :], rows[:, s0 - EARLY + k, :], ident[:, :])
                last.then_inc(s_tp, 1)

            def pe_tile(t, following=True):
                def next_transposes(*batches):
                    for g in batches if following else ():
                        transposes(t + 1, g)

                pe.wait_ge(s_early, t + 1)
                pe.wait_ge(s_dve_read, t * NB_DVE + (DENSE_READ + NB_DVE))
                pe.wait_ge(s_act_read, t * NB_ACT + NB_ACT)
                wait_reuse(pe, s_y_read, t)
                for part in range(PARTS):
                    for g in range(PER_PART):
                        for i in range(0, QUADS, PAIR):
                            p0 = QUADS * (part * PER_PART + g) + i
                            last = pe.matmul(ps_gram[PITCH * i:PITCH * (i + PAIR), part, g * COLS:(g + 1) * COLS],
                                             vecs[:, p0:p0 + PAIR, :], vecs[:, p0:p0 + PAIR, 1:SLOTS],
                                             start=True, stop=True)
                    last.then_inc(s_gram, 1)

                for bank, o0, s_read in ((ps_h_act, OC1 // 2, s_h_act_read), (ps_h_dve, 0, s_h_dve_read)):
                    wait_reuse(pe, s_read, t * (OC1 // 2))
                    for o in range(OC1 // 2):
                        pe.matmul(bank[:, o, :], w1_fold[:, (o0 + o) * P:(o0 + o + 1) * P],
                                  early[:, 0, bass.ds(t * P, P)], start=(o == 0), stop=False,
                                  skip_group_check=True)
                next_transposes(0)
                pe.wait_ge(s_fold_dve, t * PARTS + PARTS)
                pe.wait_ge(s_fold_act, t * PARTS + PARTS)
                for bank, o0, s_done in ((ps_h_act, OC1 // 2, s_h1_act), (ps_h_dve, 0, s_h1_dve)):
                    for o in range(OC1 // 2):
                        for j in range(STEPS):
                            k = PITCH * min(QUADS, FIELDS - QUADS * j)
                            last = pe.matmul(bank[:, o, :], w1_dots[0:k, j, (o0 + o) * P:(o0 + o + 1) * P],
                                             dots[0:k, j, :], start=False, stop=(j == STEPS - 1),
                                             skip_group_check=True)
                    last.then_inc(s_done, 1)
                next_transposes(1, 2)

                for c in (2, 3, 0, 1):
                    pe.wait_ge(s_h_act_read if c >= 2 else s_h_dve_read, t * 2 + (c % 2 + 1))
                    for bank, o in ((ps_h2_act, 1), (ps_h2_dve, 0)):
                        last = pe.matmul(bank, w2[:, c, o * P:(o + 1) * P], h1[:, c, :],
                                         start=(c == 2), stop=(c == 1))
                        if c == 1:
                            last.then_inc(s_h2, 1)
                next_transposes(3)

                pe.wait_ge(s_h2_dve_read, t + 1)
                pe.wait_ge(s_h2_act_read, t + 1)
                for c in range(OC2):
                    last = pe.matmul(ps_y, h2[:, c, :], w3[:, c:c + 1], start=(c == 0), stop=(c == OC2 - 1))
                last.then_inc(s_y, 1)
                next_transposes(*range(4, NB))

            for i in range(NHOT):
                pick(i)
                if i < NB:
                    transposes(0, i)
            for g in range(NHOT, NB):
                transposes(0, g)
            pe.wait_ge(s_pad, 1)
            pe.wait_ge(s_w1, 48)
            pe.wait_ge(s_w2, 48)
            pe.wait_ge(s_w1_fold, 1)
            pe_tile(0)
            with pe.Fori(1, TILES - 1) as t:
                pe_tile(t)
            pe_tile(TILES - 1, following=False)

        @block.vector
        def _(dve):
            nc.vector.memset(vecs[:, :, EARLY:PITCH], 0.0).then_inc(s_pad, 1)
            dve.wait_ge(s_row_id, 1)

            def one_hots(i):
                dve.wait_ge(s_ps_ids, i + 1)
                if i >= RING:
                    dve.wait_ge(s_picked, i - RING + 1)
                for k in KS_DVE[i]:
                    if k == 2:
                        dve.wait_ge(s_hi, i + 1)
                        nc.vector.tensor_sub(table_lo[0:KP, i], table[0:KP, i],
                                             table_hi[0:KP, i].bitcast(F32)).then_inc(s_lo, 1)
                    nc.vector.tensor_scalar(one_hot[0:KP, i % RING, k, :], ps_ids[0:KP, i % 2, :],
                                            row_id[0:KP, k:k + 1], None, ALU.is_equal).then_inc(s_hot_dve, 1)

            def read_transposed(t, g):
                dve.wait_ge(s_tp, t * NB + (g + 1))
                nc.vector.tensor_copy(slots_block(g), ps_dve[:, 0:BATCHES[g][1], :]).then_inc(s_dve_read, 1)

            one_hots(0)
            dve.wait_ge(s_dense_tp, 1)
            nc.vector.tensor_copy(early[:, 0, :], ps_dve[:, :, :].rearrange("d t p -> d (t p)")
                                  ).then_inc(s_dve_read, 1)
            one_hots(1)
            for i in range(2, NHOT):
                one_hots(i)
                if i % 2 == 0:
                    read_transposed(0, i - 2)
            dve.wait_ge(s_w1, 48)
            nc.vector.tensor_add(w1_fold[:, :], w1_dense[:, 0, :], w1_dense[:, 1, :]).then_inc(s_w1_fold, 1)
            dve.wait_ge(s_w2, 48)
            for g in range((NHOT - 1) // 2 * 2, NB, 2):
                read_transposed(0, g)

            def dve_tile(t, following=True):
                def read_next(*batches):
                    for g in batches if following else ():
                        if g % 2 == 0:
                            read_transposed(t + 1, g)

                for part in range(PARTS):
                    dve.wait_ge(s_gram, t * PARTS + (part + 1))
                    for dst, src in fold_blocks(FOLD_DVE, part):
                        last = nc.vector.tensor_copy(dst, src)
                    last.then_inc(s_fold_dve, 1)
                read_next(0)
                dve.wait_ge(s_h1_dve, t + 1)
                for o in range(OC1 // 2):
                    nc.vector.tensor_scalar(h1[:, o, :], ps_h_dve[:, o, :], b1[:, o:o + 1], 0.0,
                                            ALU.add, ALU.max).then_inc(s_h_dve_read, 1)
                read_next(1, 2)
                dve.wait_ge(s_h2, t * OC2 + OC2)
                nc.vector.tensor_scalar(h2[:, 0, :], ps_h2_dve, b2[:, 0:1], 0.0,
                                        ALU.add, ALU.max).then_inc(s_h2_dve_read, 1)
                read_next(3)
                dve.wait_ge(s_y, t + 1)
                nc.vector.tensor_copy(y[:, bass.ds(t, 1)], ps_y).then_inc(s_y_read, 1)
                read_next(*range(4, NB))

            dve_tile(0)
            with dve.Fori(1, TILES - 1) as t:
                dve_tile(t)
            dve_tile(TILES - 1, following=False)

        @block.scalar
        def _(act):
            act.wait_ge(s_row_id, 1)
            nc.scalar.mul(minus_row_id[:, :], row_id[:, :], -1.0).then_inc(s_minus, 1)

            def ids_to_psum(i):
                act.wait_ge(s_hot_ids[min(i, 1)], 16)
                if i >= 2:
                    act.wait_ge(s_hot_dve, steps_made(KS_DVE, i - 1))
                nc.scalar.copy(ps_ids[:, i % 2, :], hot_ids[:, i, :]).then_inc(s_ps_ids, 1)

            def read_picked(i):
                act.wait_ge(s_picked, i + 1)
                nc.scalar.copy(early[:, 1 + i, :], ps_pick[:, i % 2, :]).then_inc(s_pick_read, 1)

            def read_transposed(t, g):
                act.wait_ge(s_tp, t * NB + (g + 1))
                nc.scalar.copy(slots_block(g), ps_act[:, 0:BATCHES[g][1], :]).then_inc(s_act_read, 1)

            def place_early(t):
                act.wait_ge(s_gram, t * PARTS)
                nc.scalar.copy(vecs[:, :, 0:EARLY].rearrange("d p f -> d f p"),
                               early[:, :, bass.ds(t * P, P)]).then_inc(s_early, 1)

            def round_table(i):
                act.wait_ge(s_table[i], 32)
                nc.scalar.copy(table_hi[0:KP, i], table[0:KP, i]).then_inc(s_hi, 1)

            ids_to_psum(0)
            round_table(0)
            act.wait_ge(s_minus, 1)
            for i in range(NHOT):
                if i + 1 < NHOT:
                    ids_to_psum(i + 1)
                if i >= 1:
                    act.wait_ge(s_hot_act, steps_made(KS_ACT, i))
                for n, k in enumerate(KS_ACT[i]):
                    nc.scalar.activation(distance[0:KP, n, :], hot_ids[0:KP, i, :], ACT.Abs,
                                         bias=minus_row_id[0:KP, k:k + 1]).then_inc(s_distance, 1)
                if i >= RING:
                    act.wait_ge(s_picked, i - RING + 1)
                for n, k in enumerate(KS_ACT[i]):
                    act.wait_ge(s_distance, steps_made(KS_ACT, i, n + 1))
                    nc.scalar.activation(one_hot[0:KP, i % RING, k, :], distance[0:KP, n, :], ACT.Relu,
                                         bias=1.0, scale=-1.0).then_inc(s_hot_act, 1)
                if i + 1 < NHOT:
                    round_table(i + 1)
                if i >= 1:
                    read_picked(i - 1)
                if i >= 2 and i % 2 == 1:
                    read_transposed(0, i - 2)
            act.wait_ge(s_dve_read, DENSE_READ)
            act.wait_ge(s_pick_read, NHOT - 1)
            nc.scalar.copy(vecs[:, :, 0:NHOT].rearrange("d p f -> d f p"), early[:, 0:NHOT, 0:P])
            act.wait_ge(s_picked, NHOT)
            nc.scalar.copy(vecs[:, :, NHOT:EARLY].rearrange("d p f -> d (f p)"),
                           ps_pick[:, (NHOT - 1) % 2, 0:P]).then_inc(s_early, 1)
            read_picked(NHOT - 1)
            for g in range(NHOT // 2 * 2 - 1, NB, 2):
                read_transposed(0, g)
            act.wait_ge(s_pick_read, NHOT)
            act.wait_ge(s_w1, 48)
            act.wait_ge(s_w2, 48)

            def act_tile(t, following=True):
                def read_next(*batches):
                    for g in batches if following else ():
                        if g % 2 == 1:
                            read_transposed(t + 1, g)

                for part in range(PARTS):
                    act.wait_ge(s_gram, t * PARTS + (part + 1))
                    for dst, src in fold_blocks(FOLD_ACT, part):
                        last = nc.scalar.copy(dst, src)
                    last.then_inc(s_fold_act, 1)
                if following:
                    place_early(t + 1)
                act.wait_ge(s_h1_act, t + 1)
                for o in range(OC1 // 2, OC1):
                    nc.scalar.activation(h1[:, o, :], ps_h_act[:, o - OC1 // 2, :], ACT.Relu,
                                         bias=b1[:, o:o + 1]).then_inc(s_h_act_read, 1)
                read_next(1, 2)
                act.wait_ge(s_h2, t * OC2 + 1)
                nc.scalar.activation(h2[:, 1, :], ps_h2_act, ACT.Relu,
                                     bias=b2[:, 1:2]).then_inc(s_h2_act_read, 1)
                read_next(3, *range(4, NB))

            act_tile(0)
            with act.Fori(1, TILES - 1) as t:
                act_tile(t)
            act_tile(TILES - 1, following=False)


def lay_out(inputs):
    import numpy as np

    arrays = {n: np.ascontiguousarray(inputs[n])
              for n in ["r_dense_features", "ids"] + [f"tbl_{f}" for f in range(FIELDS)]}
    arrays["hot_ids"] = np.ascontiguousarray(
        arrays["ids"][:, HOT].reshape(P, TILES, NHOT).transpose(2, 1, 0).reshape(NHOT, BATCH))
    w1 = np.asarray(inputs["W_top1"])
    pairs = w1[D:D + SLOTS * (SLOTS - 1) // 2]
    row_of = {pair: r for r, pair in enumerate((a, b) for a in range(SLOTS) for b in range(a + 1, SLOTS))}
    vector = [0] + [1 + f for f in SLOT_TABLES]
    arrays["w1_dense"] = np.ascontiguousarray(np.stack([w1[:D], w1[-D:]], axis=1))
    w1_dots = np.zeros((P, STEPS, H1), w1.dtype)
    for b in range(1, SLOTS):
        j, q = divmod(b - 1, QUADS)
        for a in range(b):
            w1_dots[PITCH * q + a, j] = pairs[row_of[min(vector[a], vector[b]), max(vector[a], vector[b])]]
    arrays["w1_dots"] = w1_dots
    arrays["b_top1"] = np.ascontiguousarray(np.asarray(inputs["b_top1"]).reshape(OC1, P).T)
    arrays["b_top2"] = np.ascontiguousarray(np.asarray(inputs["b_top2"]).reshape(OC2, P).T)
    arrays["W_top2"] = np.ascontiguousarray(np.asarray(inputs["W_top2"]).reshape(OC1, P, H2).transpose(1, 0, 2))
    arrays["W_top3"] = np.ascontiguousarray(np.asarray(inputs["W_top3"]).reshape(OC2, P).T)
    return arrays


def kernel(**inputs):
    import concourse.bacc as bacc
    from concourse.bass_utils import run_bass_kernel_spmd

    nc = bacc.Bacc("TRN2", target_bir_lowering=False, num_devices=1)
    arrays = lay_out(inputs)
    ins = {n: nc.dram_tensor(f"in_{n}", a.shape, mybir.dt.from_np(a.dtype), kind="ExternalInput").ap()
           for n, a in arrays.items()}
    out = nc.dram_tensor("out_y", (BATCH, 1), F32, kind="ExternalOutput").ap()
    build(nc, ins, out)
    r = run_bass_kernel_spmd(nc, [{f"in_{n}": a for n, a in arrays.items()}], core_ids=[0])
    return r.results[0]["out_y"]
```

```python
from contextlib import ExitStack

import concourse.bass as bass
from concourse import mybir

F32 = mybir.dt.float32
F32R = mybir.dt.float32r
I32 = mybir.dt.int32
ALU = mybir.AluOpType
ACT = mybir.ActivationFunctionType

P = 128
BATCH, D, FIELDS = 512, 128, 26
H1, H2 = 512, 256
TILES = BATCH // P
SLOTS = FIELDS + 1
PITCH = 32
QUADS = P // PITCH
FIRST_B = 3
STEPS = (SLOTS - FIRST_B) // QUADS
assert STEPS * QUADS == SLOTS - FIRST_B
COPIES = 2
OC1, OC2 = H1 // P, H2 // P

HOT_ROWS = 1000
HOT = [5, 6, 7, 16, 19, 24]
NHOT = len(HOT)
KT = 8
KP = HOT_ROWS // KT
KP_A = KP // 16 * 16
KS_ACT = [[4, 5, 6] if 0 < i < NHOT - 1 else [4, 5] for i in range(NHOT)]
RUNS_DVE = [[(0, 2), (2, 4), (max(KS_ACT[i]) + 1, KT)] for i in range(NHOT)]
RING = 3
TABLE_RING = 4
EARLY = 1 + NHOT

SLOT_TABLES = HOT + [f for f in range(FIELDS) if f not in HOT]
COLD = SLOT_TABLES[NHOT:]
BATCHES, _slot = [], EARLY
for _n in [len(COLD) - 4 * 4 - 1, 4, 4, 4, 4, 1]:
    BATCHES.append((_slot, _n))
    _slot += _n
assert _slot == SLOTS
NB = len(BATCHES)
NB_DVE, NB_ACT = len(BATCHES[0::2]), len(BATCHES[1::2])
assert NB <= 2 * (NHOT - 2)

COLS = QUADS * FIELDS
PARTS = 4
BANKS = 2
PER_BANK = P // QUADS // PARTS // BANKS
BANK = 512
FOLD_DVE, FOLD_ACT = [0, 1], [2, 3]


def build(nc, ins, out):
    with ExitStack() as ctx:
        def sb(name, shape, dt=F32):
            return ctx.enter_context(nc.sbuf_tensor(name, shape, dt))

        def ps(name, shape):
            return ctx.enter_context(nc.psum_tensor(name, shape, F32))

        def sem(name):
            return ctx.enter_context(nc.semaphore(name))

        ids = sb("ids_sb", [P, TILES, FIELDS], I32)
        dense = sb("dense", [P, TILES, D])
        ident = sb("ident", [P, P])
        rows = sb("rows", [P, len(COLD), D])
        early = sb("early", [P, EARLY, BATCH])
        vecs = sb("vecs", [P, P, PITCH])
        dots = sb("dots", [P, STEPS, P])
        w1_dense = sb("w1_dense", [P, 2, H1])
        w1_fold = sb("w1_fold", [P, H1])
        w1_dots = sb("w1_dots", [P, STEPS, H1])
        w2 = sb("w2", [P, OC1, H2])
        w3 = sb("w3", [P, OC2])
        b1 = sb("b1", [P, OC1])
        b2 = sb("b2", [P, OC2])
        h1 = sb("h1", [P, OC1, P])
        h2 = sb("h2", [P, OC2, P])
        y = sb("y", [P, TILES])
        hot_ids = sb("hot_ids", [NHOT, BATCH], I32)
        hot_ids_r = sb("hot_ids_r", [NHOT, BATCH], F32R)
        ones_row = sb("ones_row", [NHOT, NHOT, P], F32R)
        table = sb("table", [P, TABLE_RING, KT, D])
        table_hi = sb("table_hi", [P, NHOT, KT, D], F32R)
        table_lo = sb("table_lo", [P, NHOT, KT, D], F32R)
        row_id = sb("row_id", [P, KT])
        minus_row_id = sb("minus_row_id", [P, KT])
        distance = sb("distance", [P, max(len(ks) for ks in KS_ACT), BATCH])
        one_hot = sb("one_hot", [P, RING, KT, BATCH], F32R)

        ps_dve = ps("ps_dve", [P, 4, P])
        ps_act = ps("ps_act", [P, 4, P])
        ps_gram = ps("ps_gram", [P, 2 * BANKS, BANK])
        ps_h_bank = ps("ps_h_bank", [P, 2, BANK])
        ps_h_dve = ps_h_bank[:, 0, 0:H1 // 2].rearrange("h (o p) -> h o p", p=P)
        ps_h_act = ps_h_bank[:, 1, 0:H1 // 2].rearrange("h (o p) -> h o p", p=P)
        ps_h2_dve, ps_h2_act = ps_gram[:, 0, 0:P], ps_gram[:, 1, 0:P]
        ps_y = ps_gram[:, 0, PER_BANK * COLS:PER_BANK * COLS + 1]
        ps_pick = ps_gram[:, 2:4, :]
        ps_ids = ps_gram[:, 0:2, :]

        s_ids = sem("s_ids")
        s_dense = sem("s_dense")
        s_hot_ids = sem("s_hot_ids")
        s_table = [sem(f"s_table{i}") for i in range(NHOT)]
        s_w1 = sem("s_w1")
        s_w2 = sem("s_w2")
        s_zero = sem("s_zero")
        s_ident = sem("s_ident")
        s_row_id = sem("s_row_id")
        s_minus = sem("s_minus")
        s_pad = sem("s_pad")
        s_w1_fold = sem("s_w1_fold")
        s_ones_row = sem("s_ones_row")
        s_hot_ids_r = sem("s_hot_ids_r")
        s_ps_ids = sem("s_ps_ids")
        s_distance = sem("s_distance")
        s_hi = sem("s_hi")
        s_lo = sem("s_lo")
        s_hot_dve = sem("s_hot_dve")
        s_hot_act = sem("s_hot_act")
        s_picked = sem("s_picked")
        s_pick_read = sem("s_pick_read")
        s_rows = [sem(f"s_rows{g}") for g in range(NB)]
        s_dense_tp = sem("s_dense_tp")
        s_tp = sem("s_tp")
        s_dve_read = sem("s_dve_read")
        s_act_read = sem("s_act_read")
        s_early = sem("s_early")
        s_gram = sem("s_gram")
        s_spare_dve = sem("s_spare_dve")
        s_spare_act = sem("s_spare_act")
        s_fold_dve = sem("s_fold_dve")
        s_fold_act = sem("s_fold_act")
        s_h1_dve = sem("s_h1_dve")
        s_h1_act = sem("s_h1_act")
        s_h2 = sem("s_h2")
        s_y = sem("s_y")
        s_h_dve_read = sem("s_h_dve_read")
        s_h_act_read = sem("s_h_act_read")
        s_h2_dve_read = sem("s_h2_dve_read")
        s_h2_act_read = sem("s_h2_act_read")
        s_y_read = sem("s_y_read")
        s_out = sem("s_out")

        DENSE_READ = 1

        def wait_reuse(eng, s, count):
            if not (isinstance(count, int) and count <= 0):
                eng.wait_ge(s, count)

        def steps_made(steps, i, n=0):
            return sum(len(x) for x in steps[:i]) + n

        def slots_block(g):
            s0, n = BATCHES[g]
            return vecs[:, :, s0:s0 + n].rearrange("d p f -> d f p")

        def fold_blocks(samples, part, quads=(), spare=False):
            src = ps_gram[:, part % 2 * BANKS:(part % 2 + 1) * BANKS, 0:PER_BANK * COLS].rearrange(
                "a k (g s c) -> a k g s c", g=PER_BANK, s=QUADS)
            dst = dots[:, :, :].rearrange("a j (h k g s) -> a h s k g j", h=PARTS, k=BANKS, g=PER_BANK)
            for s in samples:
                if spare:
                    yield (dst[0:PITCH, part, s, :, :, 0:COPIES],
                           src[PITCH * s:PITCH * (s + 1), :, :, s, 0:COPIES])
                for q in () if spare else quads:
                    rows = PITCH if q > 0 else SLOTS
                    yield (dst[PITCH * q:PITCH * q + rows, part, s],
                           src[PITCH * s:PITCH * s + rows, :, :, s, FIRST_B - 1 + q:FIELDS:QUADS])

        block = ctx.enter_context(nc.Block())

        @block.sync
        def _(sp):
            def load_table(i):
                whole = ins[f"tbl_{HOT[i]}"].rearrange("(p k) d -> p k d", k=KT)
                if i >= TABLE_RING:
                    sp.wait_ge(s_lo, i - TABLE_RING + 1)
                sp.dma_start(table[0:KP_A, i % TABLE_RING], whole[0:KP_A]).then_inc(s_table[i], 16)
                sp.dma_start(table[KP_A:KP, i % TABLE_RING], whole[KP_A:KP]).then_inc(s_table[i], 16)

            sp.dma_start(ids[:, :, :], ins["ids"].rearrange("(p t) f -> p t f", t=TILES)).then_inc(s_ids, 16)
            sp.dma_start(hot_ids[:, :], ins["hot_ids"]).then_inc(s_hot_ids, 16)
            load_table(0)
            sp.dma_start(dense[:, :, :], ins["r_dense_features"].rearrange("(p t) d -> p t d", t=TILES)
                         ).then_inc(s_dense, 16)
            load_table(1)
            for i in range(2, NHOT):
                sp.wait_ge(s_hi, i - 1)
                load_table(i)
            sp.wait_ge(s_hi, NHOT - 1)
            sp.dma_start(w1_dense[:, :, :], ins["w1_dense"]).then_inc(s_w1, 16)
            sp.dma_start(w1_dots[:, :, :], ins["w1_dots"]).then_inc(s_w1, 16)
            sp.dma_start(b1[:, :], ins["b_top1"]).then_inc(s_w1, 16)
            sp.dma_start(w2[:, :, :], ins["W_top2"]).then_inc(s_w2, 16)
            sp.dma_start(b2[:, :], ins["b_top2"]).then_inc(s_w2, 16)
            sp.dma_start(w3[:, :], ins["W_top3"]).then_inc(s_w2, 16)
            sp.wait_ge(s_y_read, TILES)
            sp.dma_start(out.rearrange("(p t) o -> p (t o)", t=TILES), y[:, :]).then_inc(s_out, 16)
            sp.wait_ge(s_out, 16)

        @block.gpsimd
        def _(pool):
            nc.gpsimd.memset(ident[:, :], 0.0).then_inc(s_zero, 1)
            nc.gpsimd.iota(row_id[:, :], [[1, KT]], base=0, channel_multiplier=KT,
                           allow_small_or_imprecise_dtypes=True).then_inc(s_row_id, 1)
            pool.wait_ge(s_zero, 1)
            nc.gpsimd.affine_select(out=ident[:, :], in_=ident[:, :], compare_op=ALU.not_equal, fill=1.0,
                                    base=0, pattern=[[-1, P]], channel_multiplier=1).then_inc(s_ident, 1)
            pool.wait_ge(s_ids, 16)
            for t in range(TILES):
                for g, (s0, n) in enumerate(BATCHES):
                    if t >= 1:
                        pool.wait_ge(s_tp, (t - 1) * NB + g + 1)
                    for slot in range(s0, s0 + n):
                        f = SLOT_TABLES[slot - 1]
                        pool.indirect_dma_start(
                            out=rows[:, slot - EARLY, :], out_offset=None, in_=ins[f"tbl_{f}"],
                            in_offset=bass.IndirectOffsetOnAxis(ap=ids[:, t, f:f + 1], axis=0),
                        ).then_inc(s_rows[g], 16)

        @block.tensor
        def _(pe):
            def spread_ids(i):
                if i >= 2:
                    pe.wait_ge(s_hot_dve, steps_made(RUNS_DVE, i - 1))
                    pe.wait_ge(s_distance, steps_made(KS_ACT, i - 1))
                for bank in (ps_ids, ps_h_bank):
                    last = pe.matmul(bank[:, i % 2, :], ones_row[:, i, :], hot_ids_r[:, :],
                                     start=True, stop=True)
                last.then_inc(s_ps_ids, 1)

            def pick(i):
                pe.wait_ge(s_hi, i + 1)
                if i >= 2:
                    pe.wait_ge(s_pick_read, i - 1)

                def products(k, part):
                    return pe.matmul(ps_pick[:, i % 2, :], part[0:KP, i, k, :], one_hot[0:KP, i % RING, k, :],
                                     start=(part is table_hi and k == 0), stop=(part is table_lo and k == KT - 1))

                for k in range(KT):
                    if k == KT // 2 and i + 2 < NHOT:
                        spread_ids(i + 2)
                    if k in KS_ACT[i]:
                        pe.wait_ge(s_hot_act, steps_made(KS_ACT, i, KS_ACT[i].index(k) + 1))
                    for n, (k0, _) in enumerate(RUNS_DVE[i]):
                        if k == k0:
                            pe.wait_ge(s_hot_dve, steps_made(RUNS_DVE, i, n + 1))
                    products(k, table_hi)
                    if k == 1:
                        pe.wait_ge(s_lo, i + 1)
                        products(0, table_lo)
                    if k >= 1:
                        last = products(k, table_lo)
                last.then_inc(s_picked, 1)

            def transposes(t, g):
                s0, n = BATCHES[g]
                pe.wait_ge(s_rows[g], t * (16 * n) + 16 * n)
                if g % 2 == 0:
                    bank = ps_dve
                    pe.wait_ge(s_dve_read, t * NB_DVE + (DENSE_READ + g // 2))
                else:
                    bank = ps_act
                    wait_reuse(pe, s_act_read, t * NB_ACT + g // 2)
                for k in range(n):
                    last = pe.transpose(bank[:, k, :], rows[:, s0 - EARLY + k, :], ident[:, :])
                last.then_inc(s_tp, 1)

            def dense_part(t, bank, o0, s_read):
                wait_reuse(pe, s_read, t * (OC1 // 2))
                for o in range(OC1 // 2):
                    pe.matmul(bank[:, o, :], w1_fold[:, (o0 + o) * P:(o0 + o + 1) * P],
                              early[:, 0, bass.ds(t * P, P)], start=(o == 0), stop=False,
                              skip_group_check=True)

            def layer_3(t):
                for c in range(OC2):
                    last = pe.matmul(ps_y, h2[:, c, :], w3[:, c:c + 1], start=(c == 0), stop=(c == OC2 - 1))
                last.then_inc(s_y, 1)

            def pe_tile(t, first=False, following=True):
                def next_transposes(*batches):
                    for g in batches if following else ():
                        transposes(t + 1, g)

                pe.wait_ge(s_dve_read, t * NB_DVE + (DENSE_READ + NB_DVE))
                pe.wait_ge(s_act_read, t * NB_ACT + NB_ACT)
                for part in range(PARTS):
                    if part == 1:
                        pe.wait_ge(s_pick_read, NHOT)
                    if part >= 2:
                        pe.wait_ge(s_fold_dve, t * PARTS + (part - 1))
                        pe.wait_ge(s_fold_act, t * PARTS + (part - 1))
                    for g in range(BANKS * PER_BANK):
                        p0 = QUADS * (part * BANKS * PER_BANK + g)
                        c0 = g % PER_BANK * COLS
                        last = pe.matmul(ps_gram[:, part % 2 * BANKS + g // PER_BANK, c0:c0 + COLS],
                                         vecs[:, p0:p0 + QUADS, :], vecs[:, p0:p0 + QUADS, 1:SLOTS],
                                         start=True, stop=True)
                    last.then_inc(s_gram, 1)
                dense_part(t, ps_h_act, OC1 // 2, s_h_act_read)
                if not first:
                    pe.wait_ge(s_fold_dve, t * PARTS + (PARTS - 1))
                    pe.wait_ge(s_fold_act, t * PARTS + (PARTS - 1))
                    layer_3(t - 1)
                next_transposes(0, 1)
                pe.wait_ge(s_fold_dve, t * PARTS + PARTS)
                pe.wait_ge(s_fold_act, t * PARTS + PARTS)
                for bank, o0, s_done in ((ps_h_act, OC1 // 2, s_h1_act), (ps_h_dve, 0, s_h1_dve)):
                    for o in range(OC1 // 2):
                        for j in range(STEPS):
                            last = pe.matmul(bank[:, o, :], w1_dots[:, j, (o0 + o) * P:(o0 + o + 1) * P],
                                             dots[:, j, :], start=False, stop=(j == STEPS - 1),
                                             skip_group_check=True)
                    last.then_inc(s_done, 1)
                next_transposes(2, 3)

                wait_reuse(pe, s_y_read, t)
                for c in (2, 3, 0, 1):
                    pe.wait_ge(s_h_act_read if c >= 2 else s_h_dve_read, t * 2 + (c % 2 + 1))
                    for bank, o in ((ps_h2_act, 1), (ps_h2_dve, 0)):
                        last = pe.matmul(bank, w2[:, c, o * P:(o + 1) * P], h1[:, c, :],
                                         start=(c == 2), stop=(c == 1))
                        if c == 1:
                            last.then_inc(s_h2, 1)
                next_transposes(*range(4, NB - 1))
                if following:
                    dense_part(t + 1, ps_h_dve, 0, s_h_dve_read)
                    pe.wait_ge(s_early, t + 2)
                    pe.wait_ge(s_h2_dve_read, t + 1)
                    pe.wait_ge(s_h2_act_read, t + 1)
                next_transposes(NB - 1)

            pe.wait_ge(s_ones_row, 1)
            pe.wait_ge(s_hot_ids_r, 1)
            spread_ids(0)
            spread_ids(1)
            pe.wait_ge(s_ident, 1)
            pe.wait_ge(s_dense, 16)
            for t in range(TILES):
                last = pe.transpose(ps_dve[:, t, :], dense[:, t, :], ident[:, :])
            last.then_inc(s_dense_tp, 1)
            for i in range(NHOT):
                pick(i)
                if i >= 1:
                    for g in range(2 * i - 2, min(2 * i, NB)):
                        transposes(0, g)
            pe.wait_ge(s_pad, 2)
            pe.wait_ge(s_w1, 48)
            pe.wait_ge(s_w2, 48)
            pe.wait_ge(s_w1_fold, 1)
            dense_part(0, ps_h_dve, 0, s_h_dve_read)
            pe.wait_ge(s_early, 1)
            pe_tile(0, first=True)
            with pe.Fori(1, TILES - 1) as t:
                pe_tile(t)
            pe_tile(TILES - 1, following=False)
            pe.wait_ge(s_h2_dve_read, TILES)
            pe.wait_ge(s_h2_act_read, TILES)
            layer_3(TILES - 1)

        @block.vector
        def _(dve):
            dve.wait_ge(s_ident, 1)
            nc.vector.tensor_copy(ones_row[:, :, :], ident[0:NHOT, 0:NHOT].unsqueeze(2).to_broadcast([NHOT, NHOT, P])
                                  ).then_inc(s_ones_row, 1)
            nc.vector.memset(vecs[:, :, SLOTS + COPIES:PITCH], 0.0).then_inc(s_pad, 1)
            nc.vector.memset(dots[0:PITCH, COPIES:STEPS, :], 0.0).then_inc(s_pad, 1)
            dve.wait_ge(s_row_id, 1)

            def one_hots(i):
                dve.wait_ge(s_ps_ids, i + 1)
                if i >= RING:
                    dve.wait_ge(s_picked, i - RING + 1)
                for n, (k0, k1) in enumerate(RUNS_DVE[i]):
                    shape = [KP, k1 - k0, BATCH]
                    nc.vector.tensor_tensor(
                        one_hot[0:KP, i % RING, k0:k1, :],
                        ps_ids[0:KP, i % 2, :].unsqueeze(1).to_broadcast(shape),
                        row_id[0:KP, k0:k1].unsqueeze(2).to_broadcast(shape), ALU.is_equal).then_inc(s_hot_dve, 1)
                    if n == 0:
                        dve.wait_ge(s_hi, i + 1)
                        nc.vector.tensor_sub(table_lo[0:KP, i], table[0:KP, i % TABLE_RING],
                                             table_hi[0:KP, i].bitcast(F32)).then_inc(s_lo, 1)
                        if i == 2:
                            dve.wait_ge(s_dense_tp, 1)
                            nc.vector.tensor_copy(early[:, 0, :], ps_dve[:, :, :].rearrange("d t p -> d (t p)")
                                                  ).then_inc(s_dve_read, 1)
                        if i >= 3:
                            read_transposed(0, 2 * (i - 3))

            def read_transposed(t, g):
                dve.wait_ge(s_tp, t * NB + (g + 1))
                nc.vector.tensor_copy(slots_block(g), ps_dve[:, 0:BATCHES[g][1], :]).then_inc(s_dve_read, 1)

            for i in range(NHOT):
                one_hots(i)
            for g in range(2 * (NHOT - 3), NB, 2):
                read_transposed(0, g)
            dve.wait_ge(s_w1, 48)
            nc.vector.tensor_add(w1_fold[:, :], w1_dense[:, 0, :], w1_dense[:, 1, :]).then_inc(s_w1_fold, 1)
            dve.wait_ge(s_w2, 48)

            def read_y(t):
                dve.wait_ge(s_y, t + 1)
                nc.vector.tensor_copy(y[:, bass.ds(t, 1)], ps_y).then_inc(s_y_read, 1)

            def dve_tile(t, first=False, following=True):
                def read_next(*batches):
                    for g in batches if following else ():
                        if g % 2 == 0:
                            read_transposed(t + 1, g)

                for part in range(PARTS):
                    dve.wait_ge(s_gram, t * PARTS + (part + 1))
                    for dst, src in fold_blocks(FOLD_DVE, part, spare=True):
                        last = nc.vector.tensor_copy(dst, src)
                    last.then_inc(s_spare_dve, 1)
                    for dst, src in fold_blocks(FOLD_DVE, part, quads=(1, 2, 3)):
                        nc.vector.tensor_copy(dst, src)
                    dve.wait_ge(s_spare_dve, t * PARTS + (part + 1))
                    for dst, src in fold_blocks(FOLD_DVE, part, quads=(0,)):
                        last = nc.vector.tensor_copy(dst, src)
                    last.then_inc(s_fold_dve, 1)
                if not first:
                    read_y(t - 1)
                read_next(0)
                dve.wait_ge(s_h1_dve, t + 1)
                for o in range(OC1 // 2):
                    nc.vector.tensor_scalar(h1[:, o, :], ps_h_dve[:, o, :], b1[:, o:o + 1], 0.0,
                                            ALU.add, ALU.max).then_inc(s_h_dve_read, 1)
                read_next(2)
                dve.wait_ge(s_h2, t * OC2 + OC2)
                nc.vector.tensor_scalar(h2[:, 0, :], ps_h2_dve, b2[:, 0:1], 0.0,
                                        ALU.add, ALU.max).then_inc(s_h2_dve_read, 1)
                read_next(*range(4, NB))

            dve_tile(0, first=True)
            with dve.Fori(1, TILES - 1) as t:
                dve_tile(t)
            dve_tile(TILES - 1, following=False)
            read_y(TILES - 1)

        @block.scalar
        def _(act):
            act.wait_ge(s_hot_ids, 16)
            nc.scalar.copy(hot_ids_r[:, :], hot_ids[:, :]).then_inc(s_hot_ids_r, 1)
            act.wait_ge(s_row_id, 1)
            nc.scalar.mul(minus_row_id[:, :], row_id[:, :], -1.0).then_inc(s_minus, 1)

            def read_picked(i):
                act.wait_ge(s_picked, i + 1)
                nc.scalar.copy(early[:, 1 + i, :], ps_pick[:, i % 2, :]).then_inc(s_pick_read, 1)

            def read_transposed(t, g):
                act.wait_ge(s_tp, t * NB + (g + 1))
                nc.scalar.copy(slots_block(g), ps_act[:, 0:BATCHES[g][1], :]).then_inc(s_act_read, 1)

            def place_copies(t):
                nc.scalar.copy(vecs[:, :, SLOTS:SLOTS + COPIES].rearrange("d p f -> d f p"),
                               early[:, 0:COPIES, bass.ds(t * P, P)])

            def place_early(t):
                act.wait_ge(s_gram, t * PARTS)
                place_copies(t)
                nc.scalar.copy(vecs[:, :, 0:EARLY].rearrange("d p f -> d f p"),
                               early[:, :, bass.ds(t * P, P)]).then_inc(s_early, 1)

            def round_table(i):
                act.wait_ge(s_table[i], 32)
                nc.scalar.copy(table_hi[0:KP, i], table[0:KP, i % TABLE_RING]).then_inc(s_hi, 1)

            round_table(0)
            act.wait_ge(s_minus, 1)
            for i in range(NHOT):
                if i >= 1:
                    act.wait_ge(s_hot_act, steps_made(KS_ACT, i))
                act.wait_ge(s_ps_ids, i + 1)
                for n, k in enumerate(KS_ACT[i]):
                    nc.scalar.activation(distance[0:KP, n, :], ps_h_bank[0:KP, i % 2, :], ACT.Abs,
                                         bias=minus_row_id[0:KP, k:k + 1]).then_inc(s_distance, 1)
                if i >= 2:
                    read_picked(i - 2)
                if i >= 3:
                    read_transposed(0, 2 * i - 5)
                if i >= RING:
                    act.wait_ge(s_picked, i - RING + 1)
                for n, k in enumerate(KS_ACT[i]):
                    act.wait_ge(s_distance, steps_made(KS_ACT, i, n + 1))
                    nc.scalar.activation(one_hot[0:KP, i % RING, k, :], distance[0:KP, n, :], ACT.Relu,
                                         bias=1.0, scale=-1.0).then_inc(s_hot_act, 1)
                if i + 1 < NHOT:
                    round_table(i + 1)
            read_picked(NHOT - 2)
            for g in range(2 * NHOT - 5, NB, 2):
                read_transposed(0, g)
            act.wait_ge(s_dve_read, DENSE_READ)
            act.wait_ge(s_pick_read, NHOT - 1)
            place_copies(0)
            nc.scalar.copy(vecs[:, :, 0:NHOT].rearrange("d p f -> d f p"), early[:, 0:NHOT, 0:P])
            act.wait_ge(s_picked, NHOT)
            nc.scalar.copy(vecs[:, :, NHOT:EARLY].rearrange("d p f -> d (f p)"),
                           ps_pick[:, (NHOT - 1) % 2, 0:P]).then_inc(s_early, 1)
            read_picked(NHOT - 1)
            act.wait_ge(s_pick_read, NHOT)
            act.wait_ge(s_w1, 48)
            act.wait_ge(s_w2, 48)

            def act_tile(t, following=True):
                def read_next(*batches):
                    for g in batches if following else ():
                        if g % 2 == 1:
                            read_transposed(t + 1, g)

                for part in range(PARTS):
                    act.wait_ge(s_gram, t * PARTS + (part + 1))
                    for dst, src in fold_blocks(FOLD_ACT, part, spare=True):
                        last = nc.scalar.copy(dst, src)
                    last.then_inc(s_spare_act, 1)
                    for dst, src in fold_blocks(FOLD_ACT, part, quads=(1, 2, 3)):
                        nc.scalar.copy(dst, src)
                    act.wait_ge(s_spare_act, t * PARTS + (part + 1))
                    for dst, src in fold_blocks(FOLD_ACT, part, quads=(0,)):
                        last = nc.scalar.copy(dst, src)
                    last.then_inc(s_fold_act, 1)
                read_next(1)
                if following:
                    place_early(t + 1)
                act.wait_ge(s_h1_act, t + 1)
                for o in range(OC1 // 2, OC1):
                    nc.scalar.activation(h1[:, o, :], ps_h_act[:, o - OC1 // 2, :], ACT.Relu,
                                         bias=b1[:, o:o + 1]).then_inc(s_h_act_read, 1)
                read_next(3)
                act.wait_ge(s_h2, t * OC2 + 1)
                nc.scalar.activation(h2[:, 1, :], ps_h2_act, ACT.Relu,
                                     bias=b2[:, 1:2]).then_inc(s_h2_act_read, 1)
                read_next(*range(5, NB))

            act_tile(0)
            with act.Fori(1, TILES - 1) as t:
                act_tile(t)
            act_tile(TILES - 1, following=False)


def lay_out(inputs):
    import numpy as np

    arrays = {n: np.ascontiguousarray(inputs[n])
              for n in ["r_dense_features", "ids"] + [f"tbl_{f}" for f in range(FIELDS)]}
    arrays["hot_ids"] = np.ascontiguousarray(
        arrays["ids"][:, HOT].reshape(P, TILES, NHOT).transpose(2, 1, 0).reshape(NHOT, BATCH))
    w1 = np.asarray(inputs["W_top1"])
    pairs = w1[D:D + SLOTS * (SLOTS - 1) // 2]
    row_of = {pair: r for r, pair in enumerate((a, b) for a in range(SLOTS) for b in range(a + 1, SLOTS))}
    vector = [0] + [1 + f for f in SLOT_TABLES]
    arrays["w1_dense"] = np.ascontiguousarray(np.stack([w1[:D], w1[-D:]], axis=1))
    w1_dots = np.zeros((P, STEPS, H1), w1.dtype)
    places = [(PITCH * ((b - FIRST_B) % QUADS) + a, (b - FIRST_B) // QUADS, a, b)
              for b in range(FIRST_B, SLOTS) for a in range(b)]
    places += [(SLOTS + a, b - 1, a, b) for b in range(1, FIRST_B) for a in range(b)]
    for p, j, a, b in places:
        w1_dots[p, j] = pairs[row_of[min(vector[a], vector[b]), max(vector[a], vector[b])]]
    arrays["w1_dots"] = w1_dots
    arrays["b_top1"] = np.ascontiguousarray(np.asarray(inputs["b_top1"]).reshape(OC1, P).T)
    arrays["b_top2"] = np.ascontiguousarray(np.asarray(inputs["b_top2"]).reshape(OC2, P).T)
    arrays["W_top2"] = np.ascontiguousarray(np.asarray(inputs["W_top2"]).reshape(OC1, P, H2).transpose(1, 0, 2))
    arrays["W_top3"] = np.ascontiguousarray(np.asarray(inputs["W_top3"]).reshape(OC2, P).T)
    return arrays


def kernel(**inputs):
    import concourse.bacc as bacc
    from concourse.bass_utils import run_bass_kernel_spmd

    nc = bacc.Bacc("TRN2", target_bir_lowering=False, num_devices=1)
    arrays = lay_out(inputs)
    ins = {n: nc.dram_tensor(f"in_{n}", a.shape, mybir.dt.from_np(a.dtype), kind="ExternalInput").ap()
           for n, a in arrays.items()}
    out = nc.dram_tensor("out_y", (BATCH, 1), F32, kind="ExternalOutput").ap()
    build(nc, ins, out)
    r = run_bass_kernel_spmd(nc, [{f"in_{n}": a for n, a in arrays.items()}], core_ids=[0])
    return r.results[0]["out_y"]
```
